# Optimizing a Trainium2 kernel written in Bass

```python
import numpy as np
import jax
import jax.numpy as jnp

def _softmax(x, axis=-1):
    return jax.nn.softmax(x, axis=axis)

def _gelu(x):
    return jax.nn.gelu(x, approximate=True)

def _silu(x):
    return jax.nn.silu(x)

def _sigmoid(x):
    return jax.nn.sigmoid(x)

def _layernorm(x, axis=-1, eps=1e-05):
    m = jnp.mean(x, axis=axis, keepdims=True)
    v = jnp.var(x, axis=axis, keepdims=True)
    return (x - m) / jnp.sqrt(v + eps)

def _scatter_add(tgt, idx, src, axis=0):
    return tgt.at[idx].add(src)

def _segment_sum(src, seg, n):
    return jax.ops.segment_sum(src, seg, n)
kernel_name = 'mk_early_fusion_d2_tok_img1024_r4_016a52'

def setup_inputs(seed: int=0):
    np.random.seed(seed)
    _w = jnp.asarray

    def _rec_inputs():
        import jax
        import jax.numpy as jnp
        _rk = jax.random.key(seed)
        x = -0.00016672 + 0.999947 * jax.random.normal(jax.random.fold_in(_rk, 1), (32, 3, 96, 96), jnp.float32)
        txt = 0.501581 + 0.625929 * jax.random.normal(jax.random.fold_in(_rk, 2), (32, 32, 256), jnp.float32)
        return (x, txt)
    x, txt = _rec_inputs()

    def _L0_tok_setup():
        import jax, jax.numpy as jnp
        import numpy as np
        key = jax.random.key(seed)
        kx, kw, kpos = jax.random.split(key, 3)
        B, C, H, W = (64, 3, 96, 96)
        p, dim = (16, 256)
        n_patches = H // p * (W // p)
        x = jax.random.normal(kx, (B, C, H, W), dtype=jnp.float32)
        w = jax.random.normal(kw, (dim, C * p * p), dtype=jnp.float32) * 0.02
        b = jnp.zeros((dim,), dtype=jnp.float32)
        cls_token = jnp.ones((dim,), dtype=jnp.float32)
        pos = jax.random.uniform(kpos, (n_patches + 1, dim), dtype=jnp.float32)
        return {'x': x, 'w': w, 'b': b, 'cls_token': cls_token, 'pos': pos, 'patch_size': p}
    _L0_tok_all = _L0_tok_setup()
    _L0_tok_in = {k: v for k, v in _L0_tok_all.items() if k in ('w', 'b', 'cls_token', 'pos')}
    del _L0_tok_all

    def _L0_attn_setup():
        import jax, jax.numpy as jnp
        import numpy as np
        B, S, D, H = (4, 512, 256, 16)
        DH = D // H
        key = jax.random.key(seed)
        ks = jax.random.split(key, 9)
        sc = 0.02
        return {'x': jax.random.normal(ks[0], (B, S, D), jnp.float32), 'WQ': jax.random.normal(ks[1], (D, D), jnp.float32) * sc, 'bQ': jax.random.normal(ks[2], (D,), jnp.float32) * sc, 'WK': jax.random.normal(ks[3], (D, D), jnp.float32) * sc, 'bK': jax.random.normal(ks[4], (D,), jnp.float32) * sc, 'WV': jax.random.normal(ks[5], (D, D), jnp.float32) * sc, 'bV': jax.random.normal(ks[6], (D,), jnp.float32) * sc, 'WO': jax.random.normal(ks[7], (DH, D), jnp.float32) * sc, 'bO': jax.random.normal(ks[8], (D,), jnp.float32) * sc}
    _L0_attn_all = _L0_attn_setup()
    _L0_attn_in = {k: v for k, v in _L0_attn_all.items() if k in ('WQ', 'bQ', 'WK', 'bK', 'WV', 'bV', 'WO', 'bO')}
    del _L0_attn_all

    def _L0_ffn_setup():
        import jax, jax.numpy as jnp
        import numpy as np
        B, S, D, H, E = (4, 512, 256, 512, 8)
        key = jax.random.key(seed)
        ks = jax.random.split(key, 8)
        scale = 0.02
        return {'x': jax.random.normal(ks[0], (B, S, D), dtype=jnp.float32), 'Wr': jax.random.normal(ks[1], (D, E), dtype=jnp.float32) * scale, 'br': jnp.zeros((E,), dtype=jnp.float32), 'W1': jax.random.normal(ks[2], (E, D, H), dtype=jnp.float32) * scale, 'b1': jnp.zeros((E, H), dtype=jnp.float32), 'W2': jax.random.normal(ks[3], (E, H, D), dtype=jnp.float32) * scale, 'b2': jnp.zeros((E, D), dtype=jnp.float32)}
    _L0_ffn_all = _L0_ffn_setup()
    _L0_ffn_in = {k: v for k, v in _L0_ffn_all.items() if k in ('Wr', 'br', 'W1', 'b1', 'W2', 'b2')}
    del _L0_ffn_all

    def _L1_attn_setup():
        import jax, jax.numpy as jnp
        import numpy as np
        D_MODEL = 256
        N_HEADS = 16
        D_HEAD = D_MODEL // N_HEADS
        key = jax.random.key(seed)
        ks = jax.random.split(key, 5)
        B, T = (4, 512)
        return {'x': jax.random.normal(ks[0], (B, T, D_MODEL), dtype=jnp.float32), 'c_attn_w': jax.random.normal(ks[1], (D_MODEL, 3 * D_MODEL), dtype=jnp.float32) * 0.02, 'c_attn_b': jax.random.normal(ks[2], (3 * D_MODEL,), dtype=jnp.float32) * 0.02, 'c_proj_w': jax.random.normal(ks[3], (D_MODEL, D_MODEL), dtype=jnp.float32) * 0.02, 'c_proj_b': jax.random.normal(ks[4], (D_MODEL,), dtype=jnp.float32) * 0.02}
    _L1_attn_all = _L1_attn_setup()
    _L1_attn_in = {k: v for k, v in _L1_attn_all.items() if k in ('c_attn_w', 'c_attn_b', 'c_proj_w', 'c_proj_b')}
    del _L1_attn_all

    def _L1_ffn_setup():
        import jax, jax.numpy as jnp
        import numpy as np
        B, S, D_MODEL, D_HIDDEN = (4, 512, 256, 1024)

        def act_quant(x):
            scale = 127.0 / jnp.clip(jnp.max(jnp.abs(x), axis=-1, keepdims=True), 1e-05)
            return jnp.clip(jnp.round(x * scale), -128, 127) / scale

        def weight_quant(w):
            scale = 1.0 / jnp.clip(jnp.mean(jnp.abs(w)), 1e-05)
            return jnp.clip(jnp.round(w * scale), -1, 1) / scale

        def bit_linear(x, w):
            xq = x + jax.lax.stop_gradient(act_quant(x) - x)
            wq = w + jax.lax.stop_gradient(weight_quant(w) - w)
            return jnp.einsum('bsd,hd->bsh', xq, wq)

        def depthwise_conv1d(x_bcl, w, b):
            y = jax.lax.conv_general_dilated(x_bcl, w, window_strides=(1,), padding=[(1, 1)], dimension_numbers=('NCH', 'OIH', 'NCH'), feature_group_count=x_bcl.shape[1])
            return y + b[None, :, None]
        key = jax.random.key(seed)
        ks = jax.random.split(key, 5)
        lim1 = 1.0 / np.sqrt(D_MODEL)
        lim2 = 1.0 / np.sqrt(D_HIDDEN)
        limc = 1.0 / np.sqrt(3.0)
        return {'x': jax.random.normal(ks[0], (B, S, D_MODEL), dtype=jnp.float32), 'w1': jax.random.uniform(ks[1], (D_HIDDEN, D_MODEL), jnp.float32, -lim1, lim1), 'conv_w': jax.random.uniform(ks[2], (D_HIDDEN, 1, 3), jnp.float32, -limc, limc), 'conv_b': jax.random.uniform(ks[3], (D_HIDDEN,), jnp.float32, -limc, limc), 'w2': jax.random.uniform(ks[4], (D_MODEL, D_HIDDEN), jnp.float32, -lim2, lim2)}
    _L1_ffn_all = _L1_ffn_setup()
    _L1_ffn_in = {k: v for k, v in _L1_ffn_all.items() if k in ('w1', 'conv_w', 'conv_b', 'w2')}
    del _L1_ffn_all
    return {'x': x, 'txt': txt, 'L0_tok_w': _L0_tok_in['w'], 'L0_tok_b': _L0_tok_in['b'], 'L0_tok_cls_token': _L0_tok_in['cls_token'], 'L0_tok_pos': _L0_tok_in['pos'], 'L0_attn_WQ': _L0_attn_in['WQ'], 'L0_attn_bQ': _L0_attn_in['bQ'], 'L0_attn_WK': _L0_attn_in['WK'], 'L0_attn_bK': _L0_attn_in['bK'], 'L0_attn_WV': _L0_attn_in['WV'], 'L0_attn_bV': _L0_attn_in['bV'], 'L0_attn_WO': _L0_attn_in['WO'], 'L0_attn_bO': _L0_attn_in['bO'], 'L0_ffn_Wr': _L0_ffn_in['Wr'], 'L0_ffn_br': _L0_ffn_in['br'], 'L0_ffn_W1': _L0_ffn_in['W1'], 'L0_ffn_b1': _L0_ffn_in['b1'], 'L0_ffn_W2': _L0_ffn_in['W2'], 'L0_ffn_b2': _L0_ffn_in['b2'], 'L1_attn_c_attn_w': _L1_attn_in['c_attn_w'], 'L1_attn_c_attn_b': _L1_attn_in['c_attn_b'], 'L1_attn_c_proj_w': _L1_attn_in['c_proj_w'], 'L1_attn_c_proj_b': _L1_attn_in['c_proj_b'], 'L1_ffn_w1': _L1_ffn_in['w1'], 'L1_ffn_conv_w': _L1_ffn_in['conv_w'], 'L1_ffn_conv_b': _L1_ffn_in['conv_b'], 'L1_ffn_w2': _L1_ffn_in['w2']}

def reference(x, txt, L0_tok_w, L0_tok_b, L0_tok_cls_token, L0_tok_pos, L0_attn_WQ, L0_attn_bQ, L0_attn_WK, L0_attn_bK, L0_attn_WV, L0_attn_bV, L0_attn_WO, L0_attn_bO, L0_ffn_Wr, L0_ffn_br, L0_ffn_W1, L0_ffn_b1, L0_ffn_W2, L0_ffn_b2, L1_attn_c_attn_w, L1_attn_c_attn_b, L1_attn_c_proj_w, L1_attn_c_proj_b, L1_ffn_w1, L1_ffn_conv_w, L1_ffn_conv_b, L1_ffn_w2):
    import jax
    import jax.numpy as jnp

    def _L0_tok_ref(x, w, b, cls_token, pos, patch_size):
        import jax, jax.numpy as jnp
        import numpy as np
        B, C, H, W = x.shape
        p = patch_size
        Hp, Wp = (H // p, W // p)
        dim = w.shape[0]
        patches = x.reshape(B, C, Hp, p, Wp, p).transpose(0, 2, 4, 1, 3, 5).reshape(B, Hp * Wp, C * p * p)
        tokens = jnp.einsum('bnf,df->bnd', patches, w) + b
        cls = jnp.broadcast_to(cls_token, (B, 1, dim))
        emb = jnp.concatenate([cls, tokens], axis=1)
        return emb + pos

    def _L0_attn_ref(x, WQ, bQ, WK, bK, WV, bV, WO, bO):
        import jax, jax.numpy as jnp
        import numpy as np
        B, S, D, H = (4, 512, 256, 16)
        DH = D // H
        b, s, d = x.shape
        h, dh = (H, DH)
        Q = (x @ WQ + bQ).reshape(b, s, h, dh).transpose(0, 2, 1, 3)
        K = (x @ WK + bK).reshape(b, s, h, dh).transpose(0, 2, 1, 3)
        V = (x @ WV + bV).reshape(b, s, h, dh).transpose(0, 2, 1, 3)
        scale = jnp.sqrt(jnp.float32(dh))
        scores = jnp.einsum('bhqd,bhkd->bhqk', Q, K) / scale
        causal = jnp.tril(jnp.ones((s, s), dtype=bool))
        scores = jnp.where(causal, scores, jnp.float32(-100000.0))
        A = jax.nn.softmax(scores, axis=-1)
        Z = jnp.einsum('bhqk,bhkd->bhqd', A, V)
        out = jnp.einsum('bhsd,de->bse', Z, WO) + jnp.float32(h) * bO
        return out

    def _L0_ffn_ref(x, Wr, br, W1, b1, W2, b2):
        import jax, jax.numpy as jnp
        import numpy as np
        B, S, D, H, E = (4, 512, 256, 512, 8)
        d = x.shape[-1]
        tokens = x.reshape(-1, d)
        logits = tokens @ Wr + br
        probs = jax.nn.softmax(logits, axis=-1)
        expert = jnp.argmax(probs, axis=-1)
        max_prob = jnp.take_along_axis(probs, expert[:, None], axis=-1)
        h = jax.nn.relu(jnp.einsum('td,edh->teh', tokens, W1) + b1[None])
        y = jnp.einsum('teh,ehd->ted', h, W2) + b2[None]
        out = jnp.take_along_axis(y, expert[:, None, None], axis=1)[:, 0, :]
        return (out * max_prob).reshape(x.shape)

    def _L1_attn_ref(x, c_attn_w, c_attn_b, c_proj_w, c_proj_b):
        import jax, jax.numpy as jnp
        import numpy as np
        D_MODEL = 256
        N_HEADS = 16
        D_HEAD = D_MODEL // N_HEADS
        B, T, D = x.shape
        H, Dh = (N_HEADS, D_HEAD)
        qkv = x @ c_attn_w + c_attn_b
        q, k, v = jnp.split(qkv, 3, axis=-1)
        q = q.reshape(B, T, H, Dh).transpose(0, 2, 1, 3)
        k = k.reshape(B, T, H, Dh).transpose(0, 2, 1, 3)
        v = v.reshape(B, T, H, Dh).transpose(0, 2, 1, 3)
        scale = Dh ** (-0.5)
        scores = jnp.einsum('bhqd,bhkd->bhqk', q, k) * scale
        causal = jnp.tril(jnp.ones((T, T), dtype=bool))
        scores = jnp.where(causal[None, None], scores, jnp.float32(-jnp.inf))
        weights = jax.nn.softmax(scores, axis=-1)
        out = jnp.einsum('bhqk,bhkd->bhqd', weights, v)
        out = out.transpose(0, 2, 1, 3).reshape(B, T, D)
        out = out @ c_proj_w + c_proj_b
        return out

    def _L1_ffn_ref(x, w1, conv_w, conv_b, w2):
        import jax, jax.numpy as jnp
        import numpy as np
        B, S, D_MODEL, D_HIDDEN = (4, 512, 256, 1024)

        def act_quant(x):
            scale = 127.0 / jnp.clip(jnp.max(jnp.abs(x), axis=-1, keepdims=True), 1e-05)
            return jnp.clip(jnp.round(x * scale), -128, 127) / scale

        def weight_quant(w):
            scale = 1.0 / jnp.clip(jnp.mean(jnp.abs(w)), 1e-05)
            return jnp.clip(jnp.round(w * scale), -1, 1) / scale

        def bit_linear(x, w):
            xq = x + jax.lax.stop_gradient(act_quant(x) - x)
            wq = w + jax.lax.stop_gradient(weight_quant(w) - w)
            return jnp.einsum('bsd,hd->bsh', xq, wq)

        def depthwise_conv1d(x_bcl, w, b):
            y = jax.lax.conv_general_dilated(x_bcl, w, window_strides=(1,), padding=[(1, 1)], dimension_numbers=('NCH', 'OIH', 'NCH'), feature_group_count=x_bcl.shape[1])
            return y + b[None, :, None]
        h = bit_linear(x, w1)
        h = depthwise_conv1d(h.transpose(0, 2, 1), conv_w, conv_b)
        h = h.transpose(0, 2, 1)
        h = jax.nn.silu(h)
        return bit_linear(h, w2)
    h = _L0_tok_ref(x, L0_tok_w, L0_tok_b, L0_tok_cls_token, L0_tok_pos, 16)
    h = jnp.concatenate([h, txt], axis=1)
    h = h + _L0_attn_ref(_layernorm(h, axis=-1), L0_attn_WQ, L0_attn_bQ, L0_attn_WK, L0_attn_bK, L0_attn_WV, L0_attn_bV, L0_attn_WO, L0_attn_bO)
    h = h + _L0_ffn_ref(_layernorm(h, axis=-1), L0_ffn_Wr, L0_ffn_br, L0_ffn_W1, L0_ffn_b1, L0_ffn_W2, L0_ffn_b2)
    h = h + _L1_attn_ref(_layernorm(h, axis=-1), L1_attn_c_attn_w, L1_attn_c_attn_b, L1_attn_c_proj_w, L1_attn_c_proj_b)
    h = h + _L1_ffn_ref(_layernorm(h, axis=-1), L1_ffn_w1, L1_ffn_conv_w, L1_ffn_conv_b, L1_ffn_w2)
    return h

_drawn_inputs = setup_inputs


def setup_inputs(seed=0):
    import zlib

    import numpy as np

    out = dict(_drawn_inputs(seed))
    spreads = {'L0_tok_b': (0.0, 0.1),
     'L0_tok_cls_token': (1.0, 0.2),
     'L0_ffn_br': (0.0, 0.3),
     'L0_ffn_b1': (0.0, 0.8),
     'L0_ffn_b2': (0.0, 0.342)}
    factors = {'L0_attn_WQ': 8.0,
     'L0_attn_bQ': 24.463,
     'L0_attn_WK': 8.0,
     'L0_attn_bK': 64.0,
     'L0_attn_bV': 6.384,
     'L0_ffn_W1': 2.751,
     'L1_attn_c_attn_b': 6.616}
    for name, (base, spread) in spreads.items():
        noise = np.random.default_rng([zlib.crc32(name.encode()), seed]).standard_normal(out[name].shape)
        drawn = base * np.exp(spread * noise) if base else spread * noise
        out[name] = jnp.asarray(drawn.astype(out[name].dtype))
    for name, factor in factors.items():
        out[name] = (out[name] * factor).astype(out[name].dtype)
    return out
```

```python
from contextlib import ExitStack

import numpy as np

import concourse.bass as bass
from concourse import mybir

F32 = mybir.dt.float32
BF16 = mybir.dt.bfloat16
I32 = mybir.dt.int32
ALU = mybir.AluOpType
ACT = mybir.ActivationFunctionType
X = mybir.AxisListType.X

B, T, D = 32, 69, 256
IMG = 37
PAIRS = B // 2
H, DH = 16, 16
KC = D // 128
FEAT = 768
FC = FEAT // 128
HPB = 128 // DH
QG = 14
NG = 5
TP = NG * QG
SR = HPB * QG
UNITS = 4
E, HID = 8, 512
HC = HID // 128
CAP = 2304
TILES = (B * T + E * 127) // 128
TPAIRS = (TILES + 1) // 2
ROWS = B * T
NO_LIST = E * CAP
HF = 1024
HFC = HF // 128
MASKED = -1e30
EPS = 1e-5
MAGIC = 1.5 * 2.0 ** 23
LAGS = 2

BANKS0 = dict(
    a=[("turn_o", 2), ("embed", 0), ("turn_x2", 2), ("logits", 2), ("turn_x", 0), ("rank", 2), ("k", 0)],
    b=[("project", 2), ("turn_e", 0), ("v", 0)],
    c=[("q", 0)],
    d=[("attend0", 1), ("attend1", 1)],
    e=[("scores0", 1), ("scores2", 1)],
    f=[("scores1", 1), ("scores3", 1)],
    g=[("turn_p0", 1), ("turn_p1", 1), ("turn_p2", 1), ("turn_p3", 1)],
)
BANKS0["h"] = BANKS0["g"]
BANKS1 = dict(
    BANKS0,
    a=[("turn_o", 2), ("turn_x2", 2), ("spread1", 2), ("turn_max", 3), ("spread2", 3), ("turn_x", 0), ("k", 0)],
    b=[("project", 2), ("ffn_out", 3), ("v", 0)],
    c=[("hidden0", 2), ("hidden1", 2), ("hidden2", 2), ("q", 0)],
)
GROUPS = [(0, 3), (3, 6), (6, 8)]
LAGS1 = 3


def live(s, lag, n):
    return not isinstance(s, int) or 0 <= s - lag < n


def reads(s, order, stage, done=False, n=PAIRS):
    at = [name for name, _ in order].index(stage) + (1 if done else 0)
    if not isinstance(s, int):
        return s * len(order) + sum((1 if k < at else 0) - lag for k, (_, lag) in enumerate(order))
    return sum(min(max(s - lag + (1 if k < at else 0), 0), n) for k, (_, lag) in enumerate(order))


def in_tiles(p, k):
    return not isinstance(p, int) or 2 * p + k < TILES


def wait(eng, sem, value):
    if not isinstance(value, int) or value > 0:
        eng.wait_ge(sem, value)


def steps(eng, n, lags, body):
    for s in range(lags + 1):
        body(s)
    with eng.Fori(lags + 1, n - 1) as s:
        body(s)
    for s in range(n - 1, n + lags):
        body(s)


class Chain:

    def __init__(self, eng, sem, item, k):
        self.eng, self.sem, self.first, self.k, self.n = eng, sem, item * k, k, 0

    def __call__(self, ins):
        self.n += 1
        ins.then_inc(self.sem, 1)
        self.eng.wait_ge(self.sem, self.first + self.n)

    def end(self):
        assert self.n == self.k, (self.n, self.k)


def program(nc, a, out):
    ctx = ExitStack()
    with ctx:
        def sb(name, shape, dt=F32):
            return ctx.enter_context(nc.sbuf_tensor(name, shape, dt))

        def sem(name):
            return ctx.enter_context(nc.semaphore(name))

        banks = {k: ctx.enter_context(nc.psum_tensor(f"bank_{k}", [128, 512], F32)) for k in "abcdefgh"}

        rows = nc.dram_tensor("expert_rows", (ROWS + 1, D), F32, kind="Internal").ap()
        lists = nc.dram_tensor("expert_lists", (E * CAP + 128, 1), I32, kind="Internal").ap()
        results = nc.dram_tensor("expert_results", (TILES * 128, D), F32, kind="Internal").ap()

        cf = sb("consts_f32", [128, CF.width])
        cb = sb("consts_bf16", [128, CB.width], BF16)
        ident = cf[:, CF.at("ident")]
        ones = cf[:, CF.at("ones")]
        head_mask = cf[:, CF.at("head_mask")]

        w_tok = sb("w_tok", [128, FC, D])
        patches = sb("patches", [128, 7680])
        patch_v = patches[:, 0:PAIRS * FC * 2 * IMG].rearrange("p (n c t) -> p n c t", n=PAIRS, c=FC)
        base_t = sb("base", [128, 2 * D])
        base, tok_bias = base_t[0:IMG, 0:D], base_t[0:IMG, D:2 * D]
        wqkv = sb("wqkv", [128, KC, 3 * D])
        wo0 = sb("wo0", [DH + 1, D])
        wo1 = sb("wo1", [128, KC, D])
        qk_bias = sb("qk_bias", [128, 2, 2, KC])
        v_bias = sb("v_bias", [T, 2, D])
        o_bias1 = sb("o_bias1", [T, D])
        wr = sb("wr", [128, KC, E])
        br = sb("br", [T, E])
        w1 = sb("w1", [128, E, KC, HID])
        w2 = sb("w2", [128, E, HC, D])
        b1 = patches[:, 0:E * HID].rearrange("p (e n) -> p e n", e=E)
        b2 = patches[:, E * HID:E * (HID + D)].rearrange("p (e n) -> p e n", e=E)
        f1 = w_tok[:].rearrange("p c n -> p (c n)")[:, 0:KC * HF // 2].bitcast(BF16).rearrange("p (c n) -> p c n", c=KC)
        f2 = sb("f2", [128, HFC, D], BF16)
        conv = sb("conv", [128, HFC, 4])

        h = sb("h", [T, B, D])
        et = sb("et", [128, KC, 2, IMG])
        xn_t = sb("xn", [128, 2 * D])
        xn = xn_t[0:T, :].rearrange("t (b d) -> t b d", b=2)
        xt = sb("xt", [128, KC, 2, TP])
        qt = sb("qt", [128, KC, 2, TP])
        kt = sb("kt", [128, KC, 2, TP])
        vv = sb("vv", [T, 2, H, DH + 1])
        qbd = [sb(f"qbd{i}", [128, NG, HPB, QG]) for i in range(2)]
        rowmax = sb("rowmax", [SR, 2, NG])
        diff_t = [sb(f"diff{i}", [128, NG * T]) for i in range(2)]
        prob_t = [sb(f"prob{i}", [128, NG * T]) for i in range(2)]
        pt_t = [sb(f"pt{i}", [128, HPB * NG * QG]) for i in range(2)]
        diff = [t[0:SR, :].rearrange("r (g k) -> r g k", g=NG) for t in diff_t]
        prob = [t[0:SR, :].rearrange("r (g k) -> r g k", g=NG) for t in prob_t]
        pt = [t[0:T, :].rearrange("t (h g q) -> t h g q", h=HPB, g=NG) for t in pt_t]
        rden = sb("rden", [T, 2, H])
        on = sb("on", [T, 2, D])
        zs = sb("zs", [T, 2, DH + 1])
        ot = sb("ot", [128, KC, 2, TP])
        stats = sb("stats", [T, 2, 2, 6])
        mv = sb("mv", [T, 2, 2, 2])
        veps = sb("veps", [T, 2, 2])
        rstd = sb("rstd", [T, 2, 2])
        x2 = sb("x2", [T, 2, D])
        x2t = sb("x2t", [128, KC, 2, TP])
        lg = sb("lg", [T, 2, E])
        lmax = sb("lmax", [T, 2])
        lrel = sb("lrel", [T, B, E])
        cand = sb("cand", [T, 2, E])
        cmax = sb("cmax", [T, 2])
        onehot = sb("onehot", [T, B, E], BF16)
        seen = sb("seen", [T, E], BF16)
        rk = sb("rk", [T, 2, E])
        slot = sb("slot", [T, B])
        slot_i = sb("slot_i", [T, 2], I32)

        thr = E * 18
        count = sb("count", [128, E])
        tiles_of = sb("tiles_of", [128, E])
        tile_end = sb("tile_end", [128, E])
        tile_start = sb("tile_start", [128, E])
        shift_e = sb("shift_e", [128, E])
        tab = xn_t[:, 0:2 * TPAIRS * E].rearrange("p (n e) -> p n e", e=E)
        tab2 = xn_t[:, 2 * TPAIRS * E:4 * TPAIRS * E].rearrange("p (n e) -> p n e", e=E)
        cols = sb("cols", [128, 4, 2 * TPAIRS])
        start_i = sb("start_i", [128, 2 * TPAIRS], I32)
        token_no = sb("token_no", [T, B], I32)
        token_i = sb("token_i", [T, 2], I32)
        expert_i = sb("expert_i", [128, 2 * TPAIRS], I32)
        gidx = sb("gidx", [128, 2], I32)
        yrow = sb("yrow", [T, B])
        yrow_i = sb("yrow_i", [T, B], I32)
        gate = sb("gate", [T, B])
        lexp = sb("lexp", [T, B, E])
        lexp_w = xn_t[0:T, 0:B * E].rearrange("t (b e) -> t b e", e=E)
        xg = [t[:, 0:D] for t in diff_t]
        ysb = [t[:, 0:D] for t in prob_t]
        hpre = [t[:].rearrange("p g h q -> p (g h q)")[:, 0:HID] for t in qbd]
        ht = [t[:, 0:HID] for t in pt_t]
        xgt = [t[:].rearrange("p c b t -> p (c b t)")[:, 0:D] for t in (x2t, ot)]
        ffn = w1[:].rearrange("p e c n -> p (e c n)")
        NW = HFC * 2 * TP
        cut = lambda i: ffn[:, i * NW:(i + 1) * NW].rearrange("p (j b t) -> p j b t", j=HFC, b=2)
        hs, yc, z = cut(0), cut(1), cut(2)
        zb = ffn[:, 3 * NW:3 * NW + NW // 2].bitcast(BF16).rearrange("p (j b t) -> p j b t", j=HFC, b=2)
        f_raw = [sb("f_raw1", [128, KC * HF]), sb("f_raw2", [128, HFC * D])]
        f_abs = sb("f_abs", [128, 2])
        f_mean = sb("f_mean", [128, 2])
        f_inv = sb("f_inv", [128, 2])
        yg = base_t[0:T, :].rearrange("t (b d) -> t b d", b=2)
        yidx = sb("yidx", [T, 2], I32)
        xq = sb("xq", [T, 2, D], BF16)
        x2tb = x2t[:].rearrange("p c b t -> p (c b t)")[:, 0:KC * TP].bitcast(BF16).rearrange("p (c b t) -> p c b t", c=KC, b=2)
        am = sb("am", [T, 2, 2])
        qs = sb("qs", [T, 4, 2])
        diag = sb("diag", [T, 2, 2, T])
        s1b = sb("s1b", [128, 2, T])
        zmax = sb("zmax", [128, 2, T])

        spare = sb("spare", [1, 384], BF16)
        spare_at = {}

        def carry_wait(eng):
            first = 0 if eng is nc.gpsimd else 192
            at = spare_at[first] = (spare_at.get(first, 0) + 1) % 192
            return eng.tensor_tensor(spare[:, first + at:first + at + 1], ones[0:1, 0:1], ones[0:1, 0:1], ALU.mult)

        consts_in = sem("consts_in")
        embed_w_in = sem("embed_w_in")
        patches_in = sem("patches_in")
        text_in = sem("text_in")
        attn0_w_in = sem("attn0_w_in")
        expert_w_in = sem("expert_w_in")
        zero_row_in = sem("zero_row_in")
        base_made = sem("base_made")
        clears_done = sem("clears_done")
        embedded = sem("embedded")
        rows_turned = sem("rows_turned")
        x2_chain = sem("x2_chain")
        logits_made = sem("logits_made")
        onehots_made = sem("onehots_made")
        route_chain = sem("route_chain")
        ranked = sem("ranked")
        slots_made = sem("slots_made")
        rows_listed = sem("rows_listed")
        NAMES = ("h_made x_made x_turned q_made k_made v_made scores_made p_turned attended o_turned projected "
                 "x2_made x2_turned var1_made rstd1_made var2_made rstd2_made qbd_made v_ready q_ready "
                 "max_made diff_made prob_made o_made rden_made ln_chain").split()
        LS = [{n: sem(f"{n}_{l}") for n in NAMES} for l in range(2)]
        BS = [{k: sem(f"bank_{k}_read_{l}") for k in "abcdefgh"} for l in range(2)]

        counted = sem("counted")
        table_chain = sem("table_chain")
        tables_made = sem("tables_made")
        gates_made = sem("gates_made")
        logits_exp = sem("logits_exp")
        ffn_w_in = sem("ffn_w_in")
        ffn_abs_made = sem("ffn_abs_made")
        ffn_abs_added = sem("ffn_abs_added")
        ffn_scales_made = sem("ffn_scales_made")
        ffn_w_chain = sem("ffn_w_chain")
        attn1_w_in = sem("attn1_w_in")
        rows_stored = sem("rows_stored")
        token_made = sem("token_made")
        gather_waited = sem("gather_waited")
        tokens_in = [sem(f"tile_tokens_in{k}") for k in range(2)]
        gathered = [sem(f"tile_gathered{k}") for k in range(2)]
        tile_turned = sem("tile_turned")
        tile_moved = sem("tile_moved")
        hid_made = sem("hid_made")
        hid_biased = sem("hid_biased")
        hid_turned = sem("hid_turned")
        hid_moved = sem("hid_moved")
        y_made = sem("y_made")
        y_biased = sem("y_biased")
        y_stored = [sem(f"tile_stored{k}") for k in range(2)]
        yidx_made = sem("yidx_made")
        y_gathered = sem("y_gathered")
        h_mixed = sem("h_mixed")
        bias_added = sem("bias_added")
        FN = ("quant_chain quantized diag1_made x2_turned_b spread1_made hidden_made conv_mid conv_prev conv_next tanh_made "
              "z_made zmax_made max_turned diag2_chain spread2_made z_scaled z_rounded ffn_made out_ready out_stored").split()
        F = {n: sem(f"ffn_{n}") for n in FN}

        block = ctx.enter_context(nc.Block())

        def tile_rows(p, k):
            return results[bass.ds(256 * p + 128 * k, 128), :]

        @block.sync
        def _(sp):
            sp.dma_start(cf[:, :], a["consts_f32"]).then_inc(consts_in, 16)
            sp.dma_start(cb[:, :], a["consts_bf16"]).then_inc(consts_in, 16)
            sp.dma_start(token_no[:], a["token_no"]).then_inc(consts_in, 16)
            sp.dma_start(w_tok[:, :, :], a["w_tok"]).then_inc(embed_w_in, 16)
            sp.dma_start(base, a["pos"]).then_inc(embed_w_in, 16)
            sp.dma_start(tok_bias[0:1, :], a["cls"].unsqueeze(0)).then_inc(embed_w_in, 16)
            sp.dma_start(tok_bias[1:IMG, :], a["tok_b"].partition_broadcast(IMG - 1)).then_inc(embed_w_in, 16)

            def load_pair(n):
                sp.dma_start(patch_v[:, bass.ds(n, 1), :, :], a["patches"][:, bass.ds(n, 1), :, :]).then_inc(patches_in, 16)
                sp.dma_start(h[IMG:T, bass.ds(2 * n, 2), :],
                             a["txt"][bass.ds(2 * n, 2)].rearrange("b t d -> t b d")).then_inc(text_in, 16)

            load_pair(0)
            for name, dst in (("wqkv0", wqkv), ("qk_bias", qk_bias)):
                sp.dma_start(dst[:], a[name]).then_inc(attn0_w_in, 16)
            sp.dma_start(v_bias[:, 0, :], a["bv0"].partition_broadcast(T)).then_inc(attn0_w_in, 16)
            sp.dma_start(v_bias[:, 1, :], a["bv1"].partition_broadcast(T)).then_inc(attn0_w_in, 16)
            sp.dma_start(wo0[0:DH, :], a["wo0"]).then_inc(attn0_w_in, 16)
            sp.dma_start(wo0[DH:DH + 1, :], a["bo0"].unsqueeze(0)).then_inc(attn0_w_in, 16)
            sp.dma_start(wr[:, :, :], a["wr"]).then_inc(attn0_w_in, 16)
            sp.dma_start(br[:, :], a["br"].partition_broadcast(T)).then_inc(attn0_w_in, 16)
            sp.dma_start(lists, a["no_tokens"]).then_inc(zero_row_in, 16)
            sp.dma_start(rows[ROWS:ROWS + 1, :], a["zero_row"]).then_inc(zero_row_in, 16)
            with sp.Fori(1, PAIRS) as n:
                sp.wait_ge(patches_in, 16 * n)
                sp.wait_ge(text_in, 16 * n)
                load_pair(n)
            sp.dma_start(w1[:], a["w1"]).then_inc(expert_w_in, 16)
            sp.dma_start(w2[:], a["w2"]).then_inc(expert_w_in, 16)
            sp.dma_start(f_raw[0][:], a["f1"].rearrange("p c n -> p (c n)")).then_inc(ffn_w_in, 16)
            sp.dma_start(f_raw[1][:], a["f2"].rearrange("p c n -> p (c n)")).then_inc(ffn_w_in, 16)
            sp.dma_start(conv[:], a["conv"]).then_inc(attn1_w_in, 16)
            sp.dma_start(wo1[:], a["wo1"]).then_inc(attn1_w_in, 16)
            sp.dma_start(o_bias1[:], a["bo1"].partition_broadcast(T)).then_inc(attn1_w_in, 16)

            def store_tokens(p):
                sp.wait_ge(LS[0]["x2_made"], 2 * p + 2)
                sp.dma_start(rows[bass.ds(2 * T * p, 2 * T), :].rearrange("(b t) d -> t b d", b=2),
                             x2[:]).then_inc(rows_stored, 16)

            with sp.Fori(0, PAIRS) as p:
                store_tokens(p)
            sp.wait_ge(rows_stored, 16 * PAIRS)
            sp.wait_ge(embedded, PAIRS)
            sp.dma_start(patches[:, 0:E * HID], a["b1"].partition_broadcast(128)).then_inc(expert_w_in, 16)
            sp.dma_start(patches[:, E * HID:E * (HID + D)], a["b2"].partition_broadcast(128)).then_inc(expert_w_in, 16)
            sp.wait_ge(LS[0]["v_made"], PAIRS)
            sp.dma_start(wqkv[:], a["wqkv1"]).then_inc(attn1_w_in, 16)

            def store_rows(p):
                sp.wait_ge(F["out_ready"], p + 1)
                sp.dma_start(out[bass.ds(2 * p, 2)].rearrange("b t d -> t b d"),
                             h[:, bass.ds(2 * p, 2), :]).then_inc(F["out_stored"], 16)

            with sp.Fori(0, PAIRS) as p:
                store_rows(p)
            sp.wait_ge(F["out_stored"], 16 * PAIRS)
            sp.wait_ge(text_in, 16 * PAIRS)
            sp.wait_ge(expert_w_in, 16 * 4)

        @block.gpsimd
        def _(pool):
            S = LS[0]
            nc.gpsimd.memset(vv[:, :, :, DH:DH + 1], 1.0).then_inc(clears_done, 1)
            nc.gpsimd.memset(xt[:, :, :, T:TP], 0.0).then_inc(clears_done, 1)
            nc.gpsimd.memset(zs[:, :, DH:DH + 1], float(H)).then_inc(clears_done, 1)
            nc.gpsimd.memset(seen[:, :], 0.0).then_inc(clears_done, 1)
            pool.wait_ge(consts_in, 48)
            pool.wait_ge(zero_row_in, 32)

            def spread_queries(S, BK, p, at):
                for u in range(UNITS):
                    b, m = u // 2, u % 2
                    pool.wait_ge(BK["c"], at)
                    wait(pool, S["scores_made"], UNITS * p + u - 1)
                    q = qt[:, m, b, :].rearrange("p (g q) -> p g q", g=NG).unsqueeze(2)
                    pool.tensor_tensor(
                        qbd[u % 2][:], q.broadcast_to([128, NG, HPB, QG]),
                        head_mask.unsqueeze(1).unsqueeze(3).broadcast_to([128, NG, HPB, QG]), ALU.mult,
                    ).then_inc(S["qbd_made"], 1)

            def inverse_deviation(S, which, made, done, p):
                wait(pool, S[made], p + 1)
                pool.tensor_tensor(veps[:, which, :], mv[:, which, :, 1], cf[0:T, CF.at("eps")], ALU.add).then_inc(S[done], 1)
                pool.wait_ge(S[done], 2 * p + 1)
                pool.tensor_tensor(rstd[:, which, :], veps[:, which, :],
                                   cf[0:T, CF.at("minus_half")], ALU.pow).then_inc(S[done], 1)

            def body(s):
                if live(s, 1, PAIRS):
                    spread_queries(S, BS[0], s - 1, reads(s - 1, BANKS0["c"], "q", done=True))
                if live(s, 2, PAIRS):
                    inverse_deviation(S, 1, "var2_made", "rstd2_made", s - 2)
                if live(s, 0, PAIRS):
                    inverse_deviation(S, 0, "var1_made", "rstd1_made", s)
                if live(s, 2, PAIRS):
                    p = s - 2
                    pool.wait_ge(slots_made, p + 1)
                    wait(pool, rows_listed, 32 * p)
                    carry_wait(pool)
                    pool.tensor_copy(token_i[:], token_no[:, bass.ds(2 * p, 2)]).then_inc(token_made, 1)
                    pool.wait_ge(token_made, p + 1)
                    carry_wait(pool)
                    for b in range(2):
                        pool.indirect_dma_start(
                            lists, bass.IndirectOffsetOnAxis(slot_i[:, b:b + 1], 0), token_i[:, b:b + 1], None,
                        ).then_inc(rows_listed, 16)

            steps(pool, PAIRS, LAGS, body)

            pool.wait_ge(rows_stored, 16 * PAIRS)

            def gather(s):
                for k in range(2):
                    if live(s, 0, TPAIRS) and in_tiles(s, k):
                        wait(pool, tokens_in[k], 16 * s + 16)
                        wait(pool, tile_turned, 2 * s + k - 1)
                        wait(pool, gather_waited, 2 * s + k)
                        carry_wait(pool).then_inc(gather_waited, 1)
                        pool.indirect_dma_start(xg[k], None, rows, bass.IndirectOffsetOnAxis(gidx[:, k:k + 1], 0)
                                                ).then_inc(gathered[k], 16)

            steps(pool, TPAIRS, 0, gather)

            fw = Chain(pool, ffn_w_chain, 0, 6)
            pool.wait_ge(ffn_scales_made, 1)
            for i, dst in enumerate((f1, f2[:])):
                raw = f_raw[i][:]
                fw(pool.tensor_scalar(raw, raw, f_inv[:, i:i + 1], MAGIC, ALU.mult, ALU.add))
                fw(pool.tensor_scalar(raw, raw, -MAGIC, 1.0, ALU.add, ALU.min))
                fw(pool.tensor_scalar(dst.rearrange("p c n -> p (c n)"), raw, -1.0, None, ALU.max))
            fw.end()

            pool.wait_ge(attn1_w_in, 16 * 4)
            for k in range(2):
                pool.wait_ge(y_stored[k], 16 * ((TILES - k + 1) // 2))
            pool.wait_ge(hid_made, TILES)
            pool.memset(x2tb[:, :, :, T:TP], 0.0).then_inc(clears_done, 1)
            S, BK, order = LS[1], BS[1], BANKS1

            def body1(s):
                if live(s, 0, PAIRS):
                    p = s
                    wait(pool, h_mixed, 2 * p)
                    carry_wait(pool)
                    pool.tensor_copy(yidx[:], yrow_i[:, bass.ds(2 * p, 2)]).then_inc(yidx_made, 1)
                    wait(pool, yidx_made, p + 1)
                    carry_wait(pool)
                    for b in range(2):
                        pool.indirect_dma_start(yg[:, b, :], None, results, bass.IndirectOffsetOnAxis(yidx[:, b:b + 1], 0)
                                                ).then_inc(y_gathered, 16)
                if live(s, 1, PAIRS):
                    spread_queries(S, BK, s - 1, reads(s - 1, order["c"], "q", done=True))
                if live(s, 2, PAIRS):
                    inverse_deviation(S, 1, "var2_made", "rstd2_made", s - 2)
                if live(s, 0, PAIRS):
                    inverse_deviation(S, 0, "var1_made", "rstd1_made", s)
                    wait(pool, S["x_made"], 2 * s + 2)
                    hp = h[:, bass.ds(2 * s, 2), :]
                    pool.tensor_tensor(hp, hp, o_bias1[:].unsqueeze(1).broadcast_to([T, 2, D]), ALU.add).then_inc(bias_added, 1)
                if live(s, 3, PAIRS):
                    p = s - 3
                    wait(pool, F["z_scaled"], p + 1)
                    wait(pool, F["ffn_made"], p)
                    carry_wait(pool)
                    pool.tensor_scalar(zb[:, :, :, 0:T], z[:, :, :, 0:T], MAGIC, -MAGIC, ALU.add, ALU.add).then_inc(F["z_rounded"], 1)

            steps(pool, PAIRS, LAGS1, body1)
            pool.wait_ge(gathered[0], 16 * ((TILES + 1) // 2))

        @block.scalar
        def _(act):
            S, BK, order = LS[0], BS[0], BANKS0
            act.wait_ge(clears_done, 4)
            act.wait_ge(attn0_w_in, 16 * 8)

            def softmax_exp(S, p, u):
                act.wait_ge(S["diff_made"], UNITS * p + u + 1)
                wait(act, S["p_turned"], UNITS * p + u - 1)
                act.activation(prob[u % 2][:], diff[u % 2][:], ACT.Exp, scale=DH ** -0.5).then_inc(S["prob_made"], 1)

            def move_pt(S, BK, p, u):
                act.wait_ge(S["p_turned"], UNITS * p + u + 1)
                wait(act, S["attended"], UNITS * p + u - 1)
                act.activation(
                    pt[u % 2][:, :, 0:4, :].rearrange("t h g q -> t g h q"),
                    banks["g"][0:T, 0:4 * SR].rearrange("t (g h q) -> t g h q", g=4, h=HPB), ACT.Copy,
                ).then_inc(BK["g"], 1)

            def move_ot(S, BK, p, L):
                act.wait_ge(S["o_turned"], p + 1)
                wait(act, S["projected"], p)
                if L == 0:
                    act.activation(ot[0:DH + 1, 0, :, 0:T],
                                   banks["a"][0:DH + 1, 0:2 * T].rearrange("p (b t) -> p b t", b=2),
                                   ACT.Copy).then_inc(BK["a"], 1)
                else:
                    act.activation(ot[:, :, :, 0:T],
                                   banks["a"][:, 0:4 * T].rearrange("p (c b t) -> p c b t", c=KC, b=2),
                                   ACT.Copy).then_inc(BK["a"], 1)

            def move_xt(S, BK, p):
                act.wait_ge(S["x_turned"], p + 1)
                wait(act, S["v_made"], p)
                act.activation(xt[:, :, :, 0:T],
                               banks["a"][:, 0:4 * T].rearrange("p (c b t) -> p c b t", c=KC, b=2),
                               ACT.Copy).then_inc(BK["a"], 1)

            def move_q(S, BK, p, L):
                act.wait_ge(S["q_made"], p + 1)
                wait(act, S["qbd_made"], UNITS * p)
                for m in range(KC):
                    ins = act.activation(qt[:, m, :, :].rearrange("p b t -> p (b t)"),
                                         banks["c"][:, m * 2 * TP:(m + 1) * 2 * TP],
                                         ACT.Identity, bias=qk_bias[:, L, 0, m:m + 1])
                ins.then_inc(BK["c"], 1)

            def body(s):
                if live(s, 2, PAIRS):
                    move_ot(S, BK, s - 2, 0)
                if live(s, 1, PAIRS):
                    softmax_exp(S, s - 1, 0)
                    softmax_exp(S, s - 1, 1)
                    move_pt(S, BK, s - 1, 0)
                if live(s, 0, PAIRS):
                    act.wait_ge(embedded, s + 1)
                    wait(act, rows_turned, s)
                    act.activation(et[:].rearrange("p c b t -> p (c b t)"), banks["a"][:, 0:KC * 2 * IMG],
                                   ACT.Copy).then_inc(BK["a"], 1)
                if live(s, 1, PAIRS):
                    softmax_exp(S, s - 1, 2)
                    move_pt(S, BK, s - 1, 1)
                    softmax_exp(S, s - 1, 3)
                    move_pt(S, BK, s - 1, 2)
                if live(s, 2, PAIRS):
                    p = s - 2
                    act.wait_ge(S["x2_turned"], p + 1)
                    wait(act, logits_made, p)
                    act.activation(x2t[:, :, :, 0:T],
                                   banks["a"][:, 0:4 * T].rearrange("p (c b t) -> p c b t", c=KC, b=2),
                                   ACT.Copy).then_inc(BK["a"], 1)
                if live(s, 1, PAIRS):
                    move_pt(S, BK, s - 1, 3)
                if live(s, 0, PAIRS):
                    move_xt(S, BK, s)
                    move_q(S, BK, s, 0)

            steps(act, PAIRS, LAGS, body)

            act.wait_ge(ffn_w_in, 32)
            for i in range(2):
                act.activation((f1, f2[:])[i].rearrange("p c n -> p (c n)"), f_raw[i][:], ACT.Abs,
                               accum_out=f_abs[:, i:i + 1]).then_inc(ffn_abs_made, 1)
            act.wait_ge(slots_made, PAIRS)
            act.activation(lexp[:], lrel[:], ACT.Exp).then_inc(logits_exp, 1)

            def move_x(t, k):
                wait(act, tile_turned, t + 1)
                wait(act, hid_made, t - 1)
                act.activation(xgt[k], banks["a"][:, 0:D], ACT.Copy).then_inc(tile_moved, 1)

            def move_hidden(t, k):
                wait(act, hid_turned, t + 1)
                wait(act, y_made, t - 1)
                act.activation(ht[k], banks["gh"[k]][:, 0:HID], ACT.Relu).then_inc(hid_moved, 1)

            act.wait_ge(rows_listed, 32 * PAIRS)
            act.wait_ge(tables_made, 1)

            def tile_tokens(p):
                for k in range(2):
                    if in_tiles(p, k):
                        at = act.value_load(start_i[0:1, bass.ds(2 * p + k, 1)], min_val=0, max_val=NO_LIST)
                        wait(act, gathered[k], 16 * p)
                        act.dma_start(gidx[:, k:k + 1], lists[bass.ds(at, 128), :]).then_inc(tokens_in[k], 16)

            def tiles(s):
                if live(s, 0, TPAIRS):
                    tile_tokens(s)
                s = s - 1
                if live(s, 1, TPAIRS):
                    p = s - 1
                    if in_tiles(p, 1):
                        move_x(2 * p + 1, 1)
                    move_hidden(2 * p, 0)
                if live(s, 2, TPAIRS):
                    for k in range(2):
                        if in_tiles(s - 2, k):
                            wait(act, y_biased, 2 * (s - 2) + k + 1)
                            act.dma_start(tile_rows(s - 2, k), ysb[k]).then_inc(y_stored[k], 16)
                if live(s, 0, TPAIRS):
                    move_x(2 * s, 0)
                if live(s, 1, TPAIRS) and in_tiles(s - 1, 1):
                    move_hidden(2 * (s - 1) + 1, 1)

            steps(act, TPAIRS, 3, tiles)

            act.wait_ge(attn1_w_in, 16 * 4)
            S, BK, order = LS[1], BS[1], BANKS1

            def middle_tap(p, g):
                j0, j1 = GROUPS[g]
                act.wait_ge(BK["c"], reads(p + 2, order["c"], f"hidden{g}", done=True))
                wait(act, F["z_made"], p)
                for j in range(j0, j1):
                    act.activation(yc[:, j, :, 0:T], hs[:, j, :, 0:T], ACT.Identity, bias=conv[:, j, 3:4],
                                   scale=conv[:, j, 1:2]).then_inc(F["conv_mid"], 1)

            def body1(s):
                if live(s, 2, PAIRS):
                    move_ot(S, BK, s - 2, 1)
                if live(s, 1, PAIRS):
                    softmax_exp(S, s - 1, 0)
                    softmax_exp(S, s - 1, 1)
                    move_pt(S, BK, s - 1, 0)
                if live(s, 3, PAIRS):
                    p = s - 3
                    wait(act, F["conv_next"], HFC * (p + 1))
                    wait(act, F["z_rounded"], p)
                    act.activation(z[:, :, :, 0:T], yc[:, :, :, 0:T], ACT.Tanh, scale=0.5).then_inc(F["tanh_made"], 1)
                if live(s, 1, PAIRS):
                    softmax_exp(S, s - 1, 2)
                    move_pt(S, BK, s - 1, 1)
                    softmax_exp(S, s - 1, 3)
                if live(s, 2, PAIRS):
                    p = s - 2
                    act.wait_ge(S["x2_turned"], p + 1)
                    wait(act, F["hidden_made"], 3 * p)
                    act.activation(x2tb[:, :, :, 0:T],
                                   banks["a"][:].bitcast(BF16)[:, 0:KC * 2 * TP].rearrange("p (c b t) -> p c b t", c=KC, b=2)[:, :, :, 0:T],
                                   ACT.Copy).then_inc(BK["a"], 1)
                if live(s, 1, PAIRS):
                    move_pt(S, BK, s - 1, 2)
                if live(s, 2, PAIRS):
                    p = s - 2
                    act.wait_ge(F["spread1_made"], p + 1)
                    wait(act, BK["c"], reads(s, order["c"], "hidden0"))
                    act.activation(s1b[:], banks["a"][:, 0:2 * T].rearrange("p (b t) -> p b t", b=2), ACT.Copy).then_inc(BK["a"], 1)
                if live(s, 1, PAIRS):
                    move_pt(S, BK, s - 1, 3)
                if live(s, 2, PAIRS):
                    middle_tap(s - 2, 0)
                    middle_tap(s - 2, 1)
                if live(s, 0, PAIRS):
                    move_xt(S, BK, s)
                    move_q(S, BK, s, 1)
                if live(s, 2, PAIRS):
                    middle_tap(s - 2, 2)

            steps(act, PAIRS, LAGS1, body1)

        @block.vector
        def _(dve):
            S, BK, order = LS[0], BS[0], BANKS0
            dve.wait_ge(consts_in, 48)
            dve.wait_ge(clears_done, 4)
            dve.wait_ge(embed_w_in, 16 * 4)
            dve.tensor_tensor(base, base, tok_bias, ALU.add).then_inc(base_made, 1)
            dve.wait_ge(base_made, 1)
            dve.wait_ge(attn0_w_in, 16 * 8)

            def norms_before(s, which):
                return reads(s, [("second", 2), ("first", 0)], ("first", "second")[which], done=True)

            def softmax_shift(S, BK, p, u):
                bank = "ef"[u % 2]
                dve.wait_ge(S["scores_made"], UNITS * p + u + 1)
                sc = banks[bank][0:SR, 0:NG * T].rearrange("r (g k) -> r g k", g=NG)
                dve.tensor_reduce(rowmax[:, u % 2, :], sc, X, ALU.max).then_inc(S["max_made"], 1)
                wait(dve, S["prob_made"], UNITS * p + u - 1)
                dve.wait_ge(S["max_made"], UNITS * p + u + 1)
                dve.tensor_tensor(diff[u % 2][:], sc, rowmax[:, u % 2, :].unsqueeze(2).broadcast_to([SR, NG, T]),
                                  ALU.subtract).then_inc(S["diff_made"], 1)

            def move_pt_rest(S, BK, p, u):
                dve.wait_ge(S["p_turned"], UNITS * p + u + 1)
                wait(dve, S["attended"], UNITS * p + u - 1)
                dve.tensor_copy(pt[u % 2][:, :, 4, :],
                                banks["h"][0:T, 0:SR].rearrange("t (h q) -> t h q", h=HPB)).then_inc(BK["h"], 1)

            def norm(S, which, src, rstd_done, var_done, p, ln_count, before_write):
                carry_wait(dve)
                for b in range(2):
                    ins = dve.bn_stats(stats[:, which, b, :], src(b))
                ins.then_inc(S["ln_chain"], 1)
                dve.wait_ge(S["ln_chain"], ln_count)
                carry_wait(dve)
                for b in range(2):
                    ins = dve.bn_aggr(mv[:, which, b, :], stats[:, which, b, :])
                ins.then_inc(S[var_done], 1)
                dve.wait_ge(S[rstd_done], 2 * p + 2)
                before_write()
                for b in range(2):
                    yield b, mv[:, which, b, 0:1], rstd[:, which, b:b + 1]

            def attend_out(S, BK, p, b, L):
                dve.wait_ge(S["attended"], UNITS * p + 2 * b + 2)
                o = banks["d"][0:T, 0:H * (DH + 1)].rearrange("t (h d) -> t h d", h=H)
                dve.reciprocal(rden[:, b, :], o[:, :, DH]).then_inc(S["rden_made"], 1)
                wait(dve, S["o_turned"], p)
                dve.wait_ge(S["rden_made"], 2 * p + b + 1)
                dve.tensor_tensor(on[:, b, :].rearrange("t (h d) -> t h d", h=H), o[:, :, 0:DH],
                                  rden[:, b, :].unsqueeze(2).broadcast_to([T, H, DH]), ALU.mult).then_inc(BK["d"], 1)
                if L == 0:
                    dve.wait_ge(BK["d"], 2 * p + b + 1)
                    dve.tensor_reduce(zs[:, b, 0:DH], on[:, b, :].rearrange("t (h d) -> t d h", h=H),
                                      X, ALU.add).then_inc(S["o_made"], 1)

            def move_k(S, BK, p, L):
                dve.wait_ge(S["k_made"], p + 1)
                wait(dve, S["scores_made"], UNITS * p)
                dve.tensor_tensor(
                    kt[:].rearrange("p m b t -> p m (b t)"), banks["a"][:, 0:KC * 2 * TP].rearrange("p (m n) -> p m n", m=KC),
                    qk_bias[:, L, 1, :].unsqueeze(2).broadcast_to([128, KC, 2 * TP]), ALU.add).then_inc(BK["a"], 1)

            def move_v(S, BK, p, L):
                dve.wait_ge(S["v_made"], p + 1)
                wait(dve, S["attended"], UNITS * p)
                dve.tensor_tensor(
                    vv[:, :, :, 0:DH], banks["b"][0:T, :].rearrange("t (b h d) -> t b h d", b=2, h=H),
                    v_bias[:, L, :].rearrange("t (h d) -> t h d", h=H).unsqueeze(1).broadcast_to([T, 2, H, DH]),
                    ALU.add).then_inc(BK["b"], 1)

            def body(s):
                if live(s, 1, PAIRS):
                    softmax_shift(S, BK, s - 1, 0)
                    softmax_shift(S, BK, s - 1, 1)
                if live(s, 2, PAIRS):
                    p = s - 2
                    dve.wait_ge(S["projected"], p + 1)
                    hp = h[:, bass.ds(2 * p, 2), :]
                    dve.tensor_tensor(hp, banks["b"][0:T, :].rearrange("t (b d) -> t b d", b=2), hp,
                                      ALU.add).then_inc(BK["b"], 1)
                    dve.wait_ge(BK["b"], reads(s, order["b"], "project", done=True))
                    dst = lambda: wait(dve, rows_stored, 16 * p)
                    for b, mean, inv in norm(S, 1, lambda b: h[:, bass.ds(2 * p + b, 1), :].rearrange("t b d -> t (b d)"),
                                             "rstd2_made", "var2_made", p, norms_before(s, 1), dst):
                        dve.tensor_scalar(x2[:, b, :], h[:, bass.ds(2 * p + b, 1), :].rearrange("t b d -> t (b d)"),
                                          mean, inv, ALU.subtract, ALU.mult).then_inc(S["x2_made"], 1)
                if live(s, 1, PAIRS):
                    move_pt_rest(S, BK, s - 1, 0)
                    softmax_shift(S, BK, s - 1, 2)
                    move_pt_rest(S, BK, s - 1, 1)
                    softmax_shift(S, BK, s - 1, 3)
                if live(s, 0, PAIRS):
                    p = s
                    dve.wait_ge(rows_turned, p + 1)
                    dve.tensor_tensor(h[0:IMG, bass.ds(2 * p, 2), :],
                                      banks["b"][0:IMG, :].rearrange("t (b d) -> t b d", b=2),
                                      base.unsqueeze(1).broadcast_to([IMG, 2, D]), ALU.add).then_inc(BK["b"], 1)
                    dve.wait_ge(text_in, 16 * p + 16)
                    dve.wait_ge(BK["b"], reads(s, order["b"], "turn_e", done=True))
                    dst = lambda: wait(dve, S["x_turned"], p)
                    for b, mean, inv in norm(S, 0, lambda b: h[:, bass.ds(2 * p + b, 1), :].rearrange("t b d -> t (b d)"),
                                             "rstd1_made", "var1_made", p, norms_before(s, 0), dst):
                        dve.tensor_scalar(xn[:, b, :], h[:, bass.ds(2 * p + b, 1), :].rearrange("t b d -> t (b d)"),
                                          mean, inv, ALU.subtract, ALU.mult).then_inc(S["x_made"], 1)
                if live(s, 1, PAIRS):
                    attend_out(S, BK, s - 1, 0, 0)
                    move_pt_rest(S, BK, s - 1, 2)
                    move_pt_rest(S, BK, s - 1, 3)
                if live(s, 2, PAIRS):
                    p = s - 2
                    c = Chain(dve, route_chain, p, 9)
                    dve.wait_ge(logits_made, p + 1)
                    at = banks["a"][0:T, 0:2 * E].rearrange("t (b e) -> t b e", b=2)
                    wide = lambda v: v.unsqueeze(2).broadcast_to([T, 2, E])
                    rows = lambda name: cf[0:T, CF.at(name)].unsqueeze(1).broadcast_to([T, 2, E])
                    dve.tensor_tensor(lg[:], at, br[:].unsqueeze(1).broadcast_to([T, 2, E]), ALU.add).then_inc(BK["a"], 1)
                    dve.wait_ge(BK["a"], reads(s, order["a"], "logits", done=True))
                    c(dve.tensor_reduce(lmax[:], lg[:], X, ALU.max))
                    c(dve.tensor_tensor(lrel[:, bass.ds(2 * p, 2), :], lg[:], wide(lmax[:]), ALU.subtract))
                    c(dve.tensor_tensor(cand[:], lg[:], wide(lmax[:]), ALU.is_equal))
                    c(dve.tensor_tensor(cand[:], cand[:], rows("countdown"), ALU.mult))
                    c(dve.tensor_reduce(cmax[:], cand[:], X, ALU.max))
                    dve.tensor_tensor(onehot[:, bass.ds(2 * p, 2), :], cand[:], wide(cmax[:]),
                                      ALU.is_equal).then_inc(onehots_made, 1)
                    dve.wait_ge(onehots_made, p + 1)
                if live(s, 1, PAIRS):
                    attend_out(S, BK, s - 1, 1, 0)
                if live(s, 2, PAIRS):
                    dve.wait_ge(ranked, p + 1)
                    dve.tensor_tensor(rk[:], at, rows("list_start"), ALU.add).then_inc(BK["a"], 1)
                    dve.wait_ge(BK["a"], reads(s, order["a"], "rank", done=True))
                    c(dve.tensor_tensor(rk[:], rk[:], onehot[:, bass.ds(2 * p, 2), :], ALU.mult))
                    c(dve.tensor_reduce(slot[:, bass.ds(2 * p, 2)], rk[:], X, ALU.add))
                    for b in range(2):
                        c(dve.tensor_tensor(seen[:], seen[:],
                                            onehot[:, bass.ds(2 * p + b, 1), :].rearrange("t b e -> t (b e)"), ALU.add))
                    wait(dve, rows_listed, 32 * p)
                    carry_wait(dve)
                    dve.tensor_copy(slot_i[:], slot[:, bass.ds(2 * p, 2)]).then_inc(slots_made, 1)
                    c.end()
                if live(s, 0, PAIRS):
                    move_k(S, BK, s, 0)
                    move_v(S, BK, s, 0)

            steps(dve, PAIRS, LAGS, body)

            c = Chain(dve, table_chain, 0, 22)
            nt = 2 * TPAIRS
            const = lambda name: cf[:, CF.at(name)]
            over_tiles = lambda v: v.unsqueeze(1).broadcast_to([128, nt, E])
            over_experts = lambda v: v.unsqueeze(2).broadcast_to([128, nt, E])
            dve.wait_ge(counted, 1)
            c(dve.tensor_copy(count[:], banks["a"][:, 0:E]))
            step = tab.rearrange("p n e -> p (n e)")[:, 0:thr].rearrange("p (e j) -> p e j", e=E)
            c(dve.tensor_tensor(step, count[:].unsqueeze(2).broadcast_to([128, E, 18]),
                                const("tile_bounds").unsqueeze(1).broadcast_to([128, E, 18]), ALU.is_gt))
            c(dve.tensor_reduce(tiles_of[:], step, X, ALU.add))
            c(dve.tensor_tensor_scan(tile_end[:], ones[:, 0:E], tiles_of[:], 0.0, ALU.mult, ALU.add))
            c(dve.tensor_tensor(tile_start[:], tile_end[:], tiles_of[:], ALU.subtract))
            c(dve.scalar_tensor_tensor(shift_e[:], tile_start[:], -128.0, const("list_start"), ALU.mult, ALU.add))
            c(dve.tensor_tensor(tab, over_experts(const("tile_no")), over_tiles(tile_end[:]), ALU.is_ge))
            c(dve.tensor_reduce(cols[:, 0, :], tab, X, ALU.add))
            c(dve.tensor_scalar(expert_i[:], cols[:, 0, :], float(E - 1), None, ALU.min))
            c(dve.tensor_tensor(tab2, over_experts(const("tile_no")), over_tiles(tile_start[:]), ALU.is_ge))
            c(dve.tensor_tensor(tab2, tab2, tab, ALU.subtract))
            c(dve.tensor_tensor(tab, tab2, over_tiles(shift_e[:]), ALU.mult))
            c(dve.tensor_reduce(cols[:, 2, :], tab, X, ALU.add))
            c(dve.tensor_scalar(cols[:, 1, :], cols[:, 0, :], float(E), None, ALU.is_lt))
            c(dve.scalar_tensor_tensor(cols[:, 2, :], const("tile_no"), 128.0, cols[:, 2, :], ALU.mult, ALU.add))
            c(dve.scalar_tensor_tensor(cols[:, 2, :], cols[:, 2, :], -float(NO_LIST), cols[:, 1, :], ALU.add, ALU.mult))
            dve.tensor_scalar(start_i[:], cols[:, 2, :], float(NO_LIST), None, ALU.add).then_inc(tables_made, 1)

            dve.wait_ge(ffn_abs_added, 1)
            c(dve.tensor_scalar(f_mean[:], banks["b"][:, 0:2], 1.0 / (D * HF), 1e-5, ALU.mult, ALU.max))
            dve.reciprocal(f_inv[:], f_mean[:]).then_inc(ffn_scales_made, 1)

            c(dve.tensor_tensor(lexp_w[:], onehot[:], shift_e[0:T].unsqueeze(1).broadcast_to([T, B, E]), ALU.mult))
            c(dve.tensor_reduce(yrow[:], lexp_w[:], X, ALU.add))
            c(dve.tensor_tensor(yrow[:], slot[:], yrow[:], ALU.subtract))
            c(dve.tensor_copy(yrow_i[:], yrow[:]))
            dve.wait_ge(logits_exp, 1)
            c(dve.tensor_reduce(gate[:], lexp[:], X, ALU.add))
            dve.reciprocal(gate[:], gate[:]).then_inc(gates_made, 1)
            c.end()

            dve.wait_ge(expert_w_in, 16 * 4)

            def expert(t):
                return dve.value_load(expert_i[0:1, bass.ds(t, 1)], min_val=0, max_val=E - 1)

            def bias_hidden(t, k):
                e = expert(t)
                wait(dve, hid_made, t + 1)
                wait(dve, hid_turned, t - 1)
                dve.tensor_tensor(hpre[k], banks["ef"[k]][:, 0:HID], b1[:, bass.ds(e, 1), :].rearrange("p e n -> p (e n)"),
                                  ALU.add).then_inc(hid_biased, 1)

            def bias_out(t, k, stored):
                e = expert(t)
                wait(dve, y_made, t + 1)
                wait(dve, y_stored[k], stored)
                dve.tensor_tensor(ysb[k], banks["cd"[k]][:, 0:D], b2[:, bass.ds(e, 1), :].rearrange("p e n -> p (e n)"),
                                  ALU.add).then_inc(y_biased, 1)

            def tiles(s):
                if live(s, 1, TPAIRS):
                    bias_hidden(2 * (s - 1), 0)
                if live(s, 2, TPAIRS) and in_tiles(s - 2, 1):
                    bias_out(2 * (s - 2) + 1, 1, 16 * (s - 2))
                if live(s, 1, TPAIRS):
                    if in_tiles(s - 1, 1):
                        bias_hidden(2 * (s - 1) + 1, 1)
                    bias_out(2 * (s - 1), 0, 16 * (s - 1))

            steps(dve, TPAIRS, 2, tiles)

            dve.wait_ge(attn1_w_in, 16 * 4)
            dve.wait_ge(ffn_w_chain, 6)
            S, BK, order = LS[1], BS[1], BANKS1

            def row_of(p, b):
                return h[:, bass.ds(2 * p + b, 1), :].rearrange("t b d -> t (b d)")

            def scale_hidden(p, g):
                j0, j1 = GROUPS[g]
                dve.wait_ge(F["hidden_made"], 3 * p + g + 1)
                if g == 0:
                    dve.wait_ge(BK["a"], reads(p + 2, order["a"], "spread1", done=True))
                wait(dve, F["conv_mid"], HFC * p)
                dve.tensor_tensor(
                    hs[:, j0:j1, :, 0:T],
                    banks["c"][:, 0:(j1 - j0) * 2 * TP].rearrange("p (j b t) -> p j b t", b=2, t=TP)[:, :, :, 0:T],
                    s1b[:].unsqueeze(1).broadcast_to([128, j1 - j0, 2, T]), ALU.mult).then_inc(BK["c"], 1)

            def outer_taps(p, g):
                for j in range(*GROUPS[g]):
                    dve.wait_ge(F["conv_mid"], HFC * p + j + 1)
                    dve.scalar_tensor_tensor(yc[:, j, :, 1:T], hs[:, j, :, 0:T - 1], conv[:, j, 0:1],
                                             yc[:, j, :, 1:T], ALU.mult, ALU.add).then_inc(F["conv_prev"], 1)
                for j in range(*GROUPS[g]):
                    dve.wait_ge(F["conv_prev"], HFC * p + j + 1)
                    dve.scalar_tensor_tensor(yc[:, j, :, 0:T - 1], hs[:, j, :, 1:T], conv[:, j, 2:3],
                                             yc[:, j, :, 0:T - 1], ALU.mult, ALU.add).then_inc(F["conv_next"], 1)

            def body1(s):
                if live(s, 1, PAIRS):
                    softmax_shift(S, BK, s - 1, 0)
                    softmax_shift(S, BK, s - 1, 1)
                if live(s, 2, PAIRS):
                    p = s - 2
                    dve.wait_ge(S["projected"], p + 1)
                    dve.wait_ge(bias_added, p + 1)
                    hp = h[:, bass.ds(2 * p, 2), :]
                    dve.tensor_tensor(hp, banks["b"][0:T, :].rearrange("t (b d) -> t b d", b=2), hp,
                                      ALU.add).then_inc(BK["b"], 1)
                    dve.wait_ge(BK["b"], reads(s, order["b"], "project", done=True))
                    for b, mean, inv in norm(S, 1, lambda b: row_of(p, b), "rstd2_made", "var2_made", p,
                                             norms_before(s, 1), lambda: None):
                        dve.tensor_scalar(x2[:, b, :], row_of(p, b), mean, inv, ALU.subtract, ALU.mult).then_inc(S["x2_made"], 1)
                    c = Chain(dve, F["quant_chain"], p, 6)
                    dve.wait_ge(S["x2_made"], 2 * p + 2)
                    c(dve.tensor_reduce(am[:, 0, :], x2[:], X, ALU.max, apply_absolute_value=True))
                    c(dve.tensor_scalar(am[:, 0, :], am[:, 0, :], 1e-5, None, ALU.max))
                    c(dve.reciprocal(qs[:, 0, :], am[:, 0, :]))
                    c(dve.tensor_scalar(qs[:, 0, :], qs[:, 0, :], 127.0, None, ALU.mult))
                    for b in range(2):
                        ins = dve.tensor_scalar(x2[:, b, :], x2[:, b, :], qs[:, 0, b:b + 1], MAGIC, ALU.mult, ALU.add)
                    c(ins)
                    wait(dve, S["x2_turned"], p)
                    dve.tensor_scalar(xq[:], x2[:], -MAGIC, 127.0, ALU.add, ALU.min).then_inc(F["quantized"], 1)
                    c(dve.tensor_scalar(qs[:, 1, :], am[:, 0, :], f_mean[0:T, 0:1], 1.0 / 127.0, ALU.mult, ALU.mult))
                    wait(dve, F["spread1_made"], p)
                    dve.tensor_tensor(diag[:, 0], ident[0:T, 0:T].unsqueeze(1).broadcast_to([T, 2, T]),
                                      qs[:, 1, :].unsqueeze(2).broadcast_to([T, 2, T]), ALU.mult).then_inc(F["diag1_made"], 1)
                    c.end()
                if live(s, 1, PAIRS):
                    move_pt_rest(S, BK, s - 1, 0)
                    softmax_shift(S, BK, s - 1, 2)
                    move_pt_rest(S, BK, s - 1, 1)
                    softmax_shift(S, BK, s - 1, 3)
                if live(s, 3, PAIRS):
                    p = s - 3
                    dve.wait_ge(F["tanh_made"], p + 1)
                    dve.scalar_tensor_tensor(z[:, :, :, 0:T].rearrange("p j b t -> p (j b) t"), z[:, :, :, 0:T].rearrange("p j b t -> p (j b) t"), 1.0,
                                             yc[:, :, :, 0:T].rearrange("p j b t -> p (j b) t"), ALU.add, ALU.mult).then_inc(F["z_made"], 1)
                    dve.wait_ge(F["z_made"], p + 1)
                    wait(dve, F["max_turned"], p)
                    dve.tensor_reduce(zmax[:], z[:, :, :, 0:T].rearrange("p j b t -> p b t j"), X, ALU.max,
                                      apply_absolute_value=True).then_inc(F["zmax_made"], 1)
                if live(s, 0, PAIRS):
                    p = s
                    dve.wait_ge(y_gathered, 32 * p + 32)
                    for b in range(2):
                        dve.scalar_tensor_tensor(row_of(p, b), yg[:, b, :], gate[:, bass.ds(2 * p + b, 1)],
                                                 row_of(p, b), ALU.mult, ALU.add).then_inc(h_mixed, 1)
                    dve.wait_ge(h_mixed, 2 * p + 2)
                    for b, mean, inv in norm(S, 0, lambda b: row_of(p, b), "rstd1_made", "var1_made", p,
                                             norms_before(s, 0), lambda: wait(dve, S["x_turned"], p)):
                        dve.tensor_scalar(xn[:, b, :], row_of(p, b), mean, inv, ALU.subtract, ALU.mult).then_inc(S["x_made"], 1)
                if live(s, 1, PAIRS):
                    attend_out(S, BK, s - 1, 0, 1)
                    move_pt_rest(S, BK, s - 1, 2)
                if live(s, 3, PAIRS):
                    p = s - 3
                    c3 = Chain(dve, F["diag2_chain"], p, 6)
                    dve.wait_ge(F["max_turned"], p + 1)
                    dve.tensor_reduce(am[:, 1, :], banks["a"][0:T, 0:256].rearrange("t (b n) -> t b n", b=2), X,
                                      ALU.max).then_inc(BK["a"], 1)
                    dve.wait_ge(BK["a"], reads(s, order["a"], "turn_max", done=True))
                    c3(dve.tensor_scalar(am[:, 1, :], am[:, 1, :], 2e-5, None, ALU.max))
                    c3(dve.reciprocal(qs[:, 2, :], am[:, 1, :]))
                    c3(dve.tensor_scalar(qs[:, 2, :], qs[:, 2, :], 127.0, None, ALU.mult))
                    c3(dve.tensor_scalar(qs[:, 3, :], am[:, 1, :], f_mean[0:T, 1:2], 1.0 / 254.0, ALU.mult, ALU.mult))
                    c3(dve.tensor_tensor(diag[:, 1], ident[0:T, 0:T].unsqueeze(1).broadcast_to([T, 2, T]),
                                         qs[:, 2, :].unsqueeze(2).broadcast_to([T, 2, T]), ALU.mult))
                if live(s, 2, PAIRS):
                    scale_hidden(s - 2, 0)
                if live(s, 1, PAIRS):
                    move_pt_rest(S, BK, s - 1, 3)
                if live(s, 3, PAIRS):
                    p = s - 3
                    dve.wait_ge(F["spread2_made"], p + 1)
                    dve.tensor_tensor(z[:, :, :, 0:T], z[:, :, :, 0:T],
                                      banks["a"][:, 0:2 * T].rearrange("p (b t) -> p b t", b=2).unsqueeze(1).broadcast_to([128, HFC, 2, T]),
                                      ALU.mult).then_inc(BK["a"], 1)
                    dve.wait_ge(BK["a"], reads(s, order["a"], "spread2", done=True))
                    carry_wait(dve).then_inc(F["z_scaled"], 1)
                if live(s, 2, PAIRS):
                    scale_hidden(s - 2, 1)
                    outer_taps(s - 2, 0)
                if live(s, 1, PAIRS):
                    attend_out(S, BK, s - 1, 1, 1)
                if live(s, 2, PAIRS):
                    scale_hidden(s - 2, 2)
                    outer_taps(s - 2, 1)
                if live(s, 0, PAIRS):
                    move_k(S, BK, s, 1)
                if live(s, 3, PAIRS):
                    p = s - 3
                    dve.wait_ge(F["ffn_made"], p + 1)
                    for b in range(2):
                        ins = dve.scalar_tensor_tensor(row_of(p, b), banks["b"][0:T, b * D:(b + 1) * D], qs[:, 3, b:b + 1],
                                                       row_of(p, b), ALU.mult, ALU.add)
                        if b == 0:
                            ins.then_inc(F["diag2_chain"], 1)
                            c3.n += 1
                    ins.then_inc(BK["b"], 1)
                    c3.end()
                    dve.wait_ge(BK["b"], reads(s, order["b"], "ffn_out", done=True))
                    carry_wait(dve).then_inc(F["out_ready"], 1)
                if live(s, 2, PAIRS):
                    outer_taps(s - 2, 2)
                if live(s, 0, PAIRS):
                    move_v(S, BK, s, 1)

            steps(dve, PAIRS, LAGS1, body1)

        @block.tensor
        def _(pe):
            mm = nc.tensor.matmul
            S, BK, order = LS[0], BS[0], BANKS0
            pe.wait_ge(consts_in, 48)
            pe.wait_ge(embed_w_in, 16 * 4)
            pe.wait_ge(attn0_w_in, 16 * 8)
            pe.wait_ge(clears_done, 4)

            def bank_free(BK, order, s, bank, stage):
                wait(pe, BK[bank], reads(s, order[bank], stage))

            def bank_moved(BK, order, s, bank, stage):
                pe.wait_ge(BK[bank], reads(s, order[bank], stage, done=True))

            def scores(S, BK, order, s, p, u):
                b, m, bank = u // 2, u % 2, "ef"[u % 2]
                pe.wait_ge(S["qbd_made"], UNITS * p + u + 1)
                if u == 0:
                    bank_moved(BK, order, s - 1, "a", "k")
                wait(pe, S["diff_made"], UNITS * p + u - 1)
                sc = banks[bank][0:SR, :]
                for g in range(NG):
                    mm(sc[:, g * T:(g + 1) * T], qbd[u % 2][:, g, :, :].rearrange("p h q -> p (h q)"),
                       kt[:, m, b, 0:T], start=True, stop=False)
                    ins = mm(sc[:, g * T:(g + 1) * T], cb[0:QG, CB.at("query_of_row")],
                             cb[0:QG, CB.at("mask")][:, g * T:(g + 1) * T], start=False, stop=True)
                ins.then_inc(S["scores_made"], 1)

            def turn_p(S, BK, order, s, p, u):
                pe.wait_ge(S["prob_made"], UNITS * p + u + 1)
                for g in range(NG):
                    bank, at = ("g", g) if g < 4 else ("h", 0)
                    if g in (0, 4):
                        bank_free(BK, order, s, bank, f"turn_p{u}")
                    ins = nc.tensor.transpose(banks[bank][0:T, at * SR:(at + 1) * SR], prob[u % 2][:, g, :],
                                              ident[0:SR, 0:SR])
                ins.then_inc(S["p_turned"], 1)

            def attend(S, BK, order, s, p, u):
                b, half = u // 2, u % 2
                bank_moved(BK, order, s, "g", f"turn_p{u}")
                bank_moved(BK, order, s, "h", f"turn_p{u}")
                if u == 0:
                    bank_moved(BK, order, s - 1, "b", "v")
                if half == 0:
                    bank_free(BK, order, s, "d", f"attend{b}")
                for i in range(HPB):
                    hd = half * HPB + i
                    ins = mm(banks["d"][0:T, hd * (DH + 1):(hd + 1) * (DH + 1)],
                             pt[u % 2][:, i, :, :].rearrange("k g q -> k (g q)")[:, 0:T],
                             vv[:, b, hd, :], start=True, stop=True)
                ins.then_inc(S["attended"], 1)

            def turn_rows(dst_bank, src):
                for b in range(2):
                    for c in range(KC):
                        at = (c * 2 + b) * T
                        ins = nc.tensor.transpose(banks[dst_bank][:, at:at + T], src[:, b, c * 128:(c + 1) * 128],
                                                  ident[0:T, 0:T])
                return ins

            def queries_or_keys(S, BK, order, s, kind):
                bank, stage = (("c", "q"), ("a", "k"))[kind]
                bank_free(BK, order, s, bank, stage)
                for m in range(KC):
                    for c in range(KC):
                        ins = mm(banks[bank][:, m * 2 * TP:(m + 1) * 2 * TP],
                                 wqkv[:, c, kind * D + m * 128:kind * D + (m + 1) * 128],
                                 xt[:, c, :, :].rearrange("p b t -> p (b t)"), start=c == 0, stop=c == KC - 1)
                ins.then_inc(S[("q_made", "k_made")[kind]], 1)

            def values(S, BK, order, s):
                bank_free(BK, order, s, "b", "v")
                for b in range(2):
                    for c in range(KC):
                        ins = mm(banks["b"][0:T, b * D:(b + 1) * D], xt[:, c, b, 0:T], wqkv[:, c, 2 * D:3 * D],
                                 start=c == 0, stop=c == KC - 1)
                ins.then_inc(S["v_made"], 1)

            def body(s):
                if live(s, 1, PAIRS):
                    scores(S, BK, order, s, s - 1, 0)
                    scores(S, BK, order, s, s - 1, 1)
                if live(s, 2, PAIRS):
                    p = s - 2
                    bank_free(BK, order, s, "a", "turn_o")
                    pe.wait_ge(S["o_made"], 2 * p + 2)
                    for b in range(2):
                        ins = nc.tensor.transpose(banks["a"][0:DH + 1, b * T:(b + 1) * T], zs[:, b, :], ident[0:T, 0:T])
                    ins.then_inc(S["o_turned"], 1)
                    bank_moved(BK, order, s, "a", "turn_o")
                    bank_free(BK, order, s, "b", "project")
                    for b in range(2):
                        ins = mm(banks["b"][0:T, b * D:(b + 1) * D], ot[0:DH + 1, 0, b, 0:T], wo0[:], start=True, stop=True)
                    ins.then_inc(S["projected"], 1)
                if live(s, 1, PAIRS):
                    turn_p(S, BK, order, s, s - 1, 0)
                    scores(S, BK, order, s, s - 1, 2)
                if live(s, 0, PAIRS):
                    pe.wait_ge(patches_in, 16 * s + 16)
                    bank_free(BK, order, s, "a", "embed")
                    for m in range(KC):
                        for c in range(FC):
                            ins = mm(banks["a"][:, m * 2 * IMG:(m + 1) * 2 * IMG], w_tok[:, c, m * 128:(m + 1) * 128],
                                     patch_v[:, bass.ds(s, 1), c, :].rearrange("p n t -> p (n t)"),
                                     start=c == 0, stop=c == FC - 1)
                    ins.then_inc(embedded, 1)
                if live(s, 1, PAIRS):
                    attend(S, BK, order, s, s - 1, 0)
                    turn_p(S, BK, order, s, s - 1, 1)
                    scores(S, BK, order, s, s - 1, 3)
                if live(s, 0, PAIRS):
                    bank_moved(BK, order, s, "a", "embed")
                    bank_free(BK, order, s, "b", "turn_e")
                    mm(banks["b"][:, 0:1], cb[:, CB.at("ones")], cb[:, CB.at("ones")][:, 0:1], start=True, stop=True)
                    for b in range(2):
                        for c in range(KC):
                            ins = nc.tensor.transpose(banks["b"][0:IMG, b * D + c * 128:b * D + (c + 1) * 128],
                                                      et[:, c, b, :], ident)
                    ins.then_inc(rows_turned, 1)
                if live(s, 1, PAIRS):
                    attend(S, BK, order, s, s - 1, 1)
                    turn_p(S, BK, order, s, s - 1, 2)
                if live(s, 2, PAIRS):
                    pe.wait_ge(S["x2_made"], 2 * (s - 2) + 2)
                    bank_free(BK, order, s, "a", "turn_x2")
                    turn_rows("a", x2).then_inc(S["x2_turned"], 1)
                if live(s, 1, PAIRS):
                    attend(S, BK, order, s, s - 1, 2)
                    turn_p(S, BK, order, s, s - 1, 3)
                if live(s, 2, PAIRS):
                    bank_moved(BK, order, s, "a", "turn_x2")
                    for b in range(2):
                        for c in range(KC):
                            ins = mm(banks["a"][0:T, b * E:(b + 1) * E], x2t[:, c, b, 0:T], wr[:, c, :],
                                     start=c == 0, stop=c == KC - 1)
                    ins.then_inc(logits_made, 1)
                if live(s, 0, PAIRS):
                    bank_free(BK, order, s, "a", "turn_x")
                    pe.wait_ge(S["x_made"], 2 * s + 2)
                    turn_rows("a", xn).then_inc(S["x_turned"], 1)
                if live(s, 1, PAIRS):
                    attend(S, BK, order, s, s - 1, 3)
                if live(s, 2, PAIRS):
                    p = s - 2
                    pe.wait_ge(onehots_made, p + 1)
                    wait(pe, slots_made, p)
                    bank_free(BK, order, s, "a", "rank")
                    before, every = cb[0:T, CB.at("before")], cb[0:T, CB.at("ones")][:, 0:T]
                    oh = lambda b: onehot[:, bass.ds(2 * p + b, 1), :].rearrange("t b e -> t (b e)")
                    rank = lambda b: banks["a"][0:T, b * E:(b + 1) * E]
                    mm(rank(0), before, oh(0), start=True, stop=False)
                    mm(rank(0), every, seen[:], start=False, stop=True)
                    mm(rank(1), before, oh(1), start=True, stop=False)
                    mm(rank(1), every, oh(0), start=False, stop=False)
                    mm(rank(1), every, seen[:], start=False, stop=True).then_inc(ranked, 1)
                if live(s, 0, PAIRS):
                    bank_moved(BK, order, s, "a", "turn_x")
                    queries_or_keys(S, BK, order, s, 0)
                    queries_or_keys(S, BK, order, s, 1)
                    values(S, BK, order, s)

            steps(pe, PAIRS, LAGS, body)

            pe.wait_ge(slots_made, PAIRS)
            mm(banks["a"][:, 0:E], cb[0:T, CB.at("ones")], seen[:], start=True, stop=True).then_inc(counted, 1)
            pe.wait_ge(ffn_abs_made, 2)
            bank_free(BK, order, PAIRS + LAGS, "b", "project")
            mm(banks["b"][:, 0:2], ones, f_abs[:], start=True, stop=True).then_inc(ffn_abs_added, 1)

            pe.wait_ge(expert_w_in, 16 * 4)
            pe.wait_ge(tables_made, 1)
            pe.wait_ge(table_chain, 9)

            def expert(t):
                return pe.value_load(expert_i[0:1, bass.ds(t, 1)], min_val=0, max_val=E - 1)

            def turn_tile(t, k, loads):
                wait(pe, gathered[k], loads)
                wait(pe, tile_moved, t)
                for c in range(KC):
                    ins = nc.tensor.transpose(banks["a"][:, c * 128:(c + 1) * 128], xg[k][:, c * 128:(c + 1) * 128], ident)
                ins.then_inc(tile_turned, 1)

            def hidden(t, k):
                e = expert(t)
                wait(pe, tile_moved, t + 1)
                wait(pe, hid_biased, t - 1)
                for c in range(KC):
                    ins = mm(banks["ef"[k]][:, 0:HID], xgt[k][:, c * 128:(c + 1) * 128],
                             w1[:, bass.ds(e, 1), c, :].rearrange("p e n -> p (e n)"), start=c == 0, stop=c == KC - 1)
                ins.then_inc(hid_made, 1)

            def turn_hidden(t, k):
                wait(pe, hid_biased, t + 1)
                wait(pe, hid_moved, t - 1)
                for c in range(HC):
                    ins = nc.tensor.transpose(banks["gh"[k]][:, c * 128:(c + 1) * 128], hpre[k][:, c * 128:(c + 1) * 128], ident)
                ins.then_inc(hid_turned, 1)

            def result(t, k):
                e = expert(t)
                wait(pe, hid_moved, t + 1)
                wait(pe, y_biased, t - 1)
                for c in range(HC):
                    ins = mm(banks["cd"[k]][:, 0:D], ht[k][:, c * 128:(c + 1) * 128],
                             w2[:, bass.ds(e, 1), c, :].rearrange("p e n -> p (e n)"), start=c == 0, stop=c == HC - 1)
                ins.then_inc(y_made, 1)

            def tiles(s):
                if live(s, 1, TPAIRS):
                    p = s - 1
                    hidden(2 * p, 0)
                    if in_tiles(p, 1):
                        turn_tile(2 * p + 1, 1, 16 * (p + 1))
                if live(s, 2, TPAIRS) and in_tiles(s - 2, 1):
                    result(2 * (s - 2) + 1, 1)
                if live(s, 1, TPAIRS):
                    turn_hidden(2 * (s - 1), 0)
                    if in_tiles(s - 1, 1):
                        hidden(2 * (s - 1) + 1, 1)
                if live(s, 0, TPAIRS):
                    turn_tile(2 * s, 0, 16 * (s + 1))
                if live(s, 1, TPAIRS):
                    result(2 * (s - 1), 0)
                    if in_tiles(s - 1, 1):
                        turn_hidden(2 * (s - 1) + 1, 1)

            steps(pe, TPAIRS, 2, tiles)

            S, BK, order = LS[1], BS[1], BANKS1
            pe.wait_ge(attn1_w_in, 16 * 4)
            pe.wait_ge(clears_done, 5)
            pe.wait_ge(ffn_w_chain, 6)
            pe.wait_ge(y_biased, TILES)

            def spread(bank_cols, rows):
                return mm(bank_cols, ones[0:T, :], rows.rearrange("t b n -> t (b n)"), start=True, stop=True)

            def hidden_group(p, g, s):
                bank_free(BK, order, s, "c", f"hidden{g}")
                j0, j1 = GROUPS[g]
                for j in range(j0, j1):
                    for c in range(KC):
                        ins = mm(banks["c"][:, (j - j0) * 2 * TP:(j - j0 + 1) * 2 * TP], f1[:, c, j * 128:(j + 1) * 128],
                                 x2tb[:, c, :, :].rearrange("p b t -> p (b t)"), start=c == 0, stop=c == KC - 1)
                ins.then_inc(F["hidden_made"], 1)

            def body1(s):
                if live(s, 1, PAIRS):
                    scores(S, BK, order, s, s - 1, 0)
                    scores(S, BK, order, s, s - 1, 1)
                if live(s, 2, PAIRS):
                    p = s - 2
                    bank_free(BK, order, s, "a", "turn_o")
                    pe.wait_ge(BK["d"], reads(s - 1, order["d"], "attend1", done=True))
                    turn_rows("a", on).then_inc(S["o_turned"], 1)
                    bank_moved(BK, order, s, "a", "turn_o")
                    bank_free(BK, order, s, "b", "project")
                    for b in range(2):
                        for c in range(KC):
                            ins = mm(banks["b"][0:T, b * D:(b + 1) * D], ot[:, c, b, 0:T], wo1[:, c, :],
                                     start=c == 0, stop=c == KC - 1)
                    ins.then_inc(S["projected"], 1)
                if live(s, 1, PAIRS):
                    turn_p(S, BK, order, s, s - 1, 0)
                    scores(S, BK, order, s, s - 1, 2)
                    attend(S, BK, order, s, s - 1, 0)
                    turn_p(S, BK, order, s, s - 1, 1)
                    scores(S, BK, order, s, s - 1, 3)
                if live(s, 2, PAIRS):
                    p = s - 2
                    pe.wait_ge(F["quantized"], p + 1)
                    bank_free(BK, order, s, "a", "turn_x2")
                    at = banks["a"][:].bitcast(BF16)
                    for b in range(2):
                        for c in range(KC):
                            o = (c * 2 + b) * TP
                            ins = nc.tensor.transpose(at[:, o:o + T], xq[:, b, c * 128:(c + 1) * 128],
                                                      cb[0:T, CB.at("ident")][:, 0:T])
                    ins.then_inc(S["x2_turned"], 1)
                if live(s, 1, PAIRS):
                    attend(S, BK, order, s, s - 1, 1)
                    turn_p(S, BK, order, s, s - 1, 2)
                if live(s, 2, PAIRS):
                    p = s - 2
                    pe.wait_ge(F["diag1_made"], p + 1)
                    bank_free(BK, order, s, "a", "spread1")
                    spread(banks["a"][:, 0:2 * T], diag[:, 0]).then_inc(F["spread1_made"], 1)
                if live(s, 3, PAIRS):
                    p = s - 3
                    pe.wait_ge(F["zmax_made"], p + 1)
                    bank_free(BK, order, s, "a", "turn_max")
                    for b in range(2):
                        ins = nc.tensor.transpose(banks["a"][0:T, b * 128:(b + 1) * 128], zmax[:, b, :], ident)
                    ins.then_inc(F["max_turned"], 1)
                if live(s, 2, PAIRS):
                    hidden_group(s - 2, 0, s)
                if live(s, 1, PAIRS):
                    attend(S, BK, order, s, s - 1, 2)
                    turn_p(S, BK, order, s, s - 1, 3)
                if live(s, 3, PAIRS):
                    p = s - 3
                    pe.wait_ge(F["diag2_chain"], 6 * p + 5)
                    bank_free(BK, order, s, "a", "spread2")
                    spread(banks["a"][:, 0:2 * T], diag[:, 1]).then_inc(F["spread2_made"], 1)
                if live(s, 2, PAIRS):
                    hidden_group(s - 2, 1, s)
                if live(s, 0, PAIRS):
                    bank_free(BK, order, s, "a", "turn_x")
                    pe.wait_ge(S["x_made"], 2 * s + 2)
                    turn_rows("a", xn).then_inc(S["x_turned"], 1)
                if live(s, 1, PAIRS):
                    attend(S, BK, order, s, s - 1, 3)
                if live(s, 2, PAIRS):
                    hidden_group(s - 2, 2, s)
                if live(s, 0, PAIRS):
                    bank_moved(BK, order, s, "a", "turn_x")
                    queries_or_keys(S, BK, order, s, 0)
                    queries_or_keys(S, BK, order, s, 1)
                if live(s, 3, PAIRS):
                    p = s - 3
                    pe.wait_ge(F["z_rounded"], p + 1)
                    bank_free(BK, order, s, "b", "ffn_out")
                    for b in range(2):
                        for j in range(HFC):
                            ins = mm(banks["b"][0:T, b * D:(b + 1) * D], zb[:, j, b, 0:T], f2[:, j, :],
                                     start=j == 0, stop=j == HFC - 1)
                    ins.then_inc(F["ffn_made"], 1)
                if live(s, 0, PAIRS):
                    values(S, BK, order, s)

            steps(pe, PAIRS, LAGS1, body1)


class Columns:

    def __init__(self, **parts):
        self.parts = {k: np.asarray(v, np.float32) for k, v in parts.items()}
        self.width, self.where = 0, {}
        for k, v in self.parts.items():
            self.where[k] = slice(self.width, self.width + v.shape[1])
            self.width += v.shape[1]

    def at(self, name):
        return self.where[name]

    def tile(self):
        t = np.zeros((128, self.width), np.float32)
        for k, v in self.parts.items():
            t[0:v.shape[0], self.where[k]] = v
        return t


def rows_of(v, n=128):
    return np.broadcast_to(np.asarray(v, np.float32)[None, :], (n, len(v)))


_p = np.arange(128)
CF = Columns(
    ident=np.eye(128),
    ones=np.ones((128, 128)),
    head_mask=_p[:, None] // DH == np.arange(HPB)[None, :],
    minus_half=np.full((128, 2), -0.5),
    eps=np.full((128, 2), EPS),
    countdown=rows_of(E - np.arange(E)),
    list_start=rows_of(CAP * np.arange(E)),
    tile_bounds=rows_of(128 * np.arange(18)),
    tile_no=rows_of(np.arange(2 * TPAIRS)),
)
_r = np.arange(QG)
CB = Columns(
    query_of_row=_r[:, None] == np.tile(_r, HPB)[None, :],
    mask=np.where(np.arange(T)[None, None, :] > QG * np.arange(NG)[None, :, None] + _r[:, None, None],
                  MASKED, 0.0).reshape(QG, NG * T),
    before=np.arange(T)[:, None] < np.arange(T)[None, :],
    ones=np.ones((128, 128)),
    ident=np.eye(128),
)


def laid_out(x):
    f = np.asarray
    p16 = 16
    img = f(x["x"]).reshape(B, 3, 6, p16, 6, p16).transpose(1, 3, 5, 0, 2, 4).reshape(FC, 128, PAIRS, 2, IMG - 1)
    patches = np.zeros((128, PAIRS, FC, 2, IMG), np.float32)
    patches[..., 1:] = img.transpose(1, 2, 0, 3, 4)
    chunks = lambda w: np.ascontiguousarray(f(w).reshape(-1, 128, f(w).shape[-1]).transpose(1, 0, 2))
    cols = lambda v: f(v).reshape(-1, 128).T
    qkvb = f(x["L1_attn_c_attn_b"])
    return {
        "consts_f32": CF.tile(),
        "consts_bf16": CB.tile().astype(mybir.dt.np(BF16)),
        "zero_row": np.zeros((1, D), np.float32),
        "no_tokens": np.full((E * CAP + 128, 1), ROWS, np.int32),
        "token_no": (T * np.arange(B)[None, :] + np.arange(T)[:, None]).astype(np.int32),
        "patches": patches.reshape(128, PAIRS, FC, 2 * IMG),
        "txt": f(x["txt"]),
        "w_tok": chunks(f(x["L0_tok_w"]).T),
        "pos": f(x["L0_tok_pos"]),
        "cls": f(x["L0_tok_cls_token"]),
        "tok_b": f(x["L0_tok_b"]),
        "wqkv0": chunks(np.concatenate([f(x["L0_attn_WQ"]), f(x["L0_attn_WK"]), f(x["L0_attn_WV"])], axis=1)),
        "wqkv1": chunks(x["L1_attn_c_attn_w"]),
        "qk_bias": np.ascontiguousarray(np.stack(
            [np.stack([cols(x["L0_attn_bQ"]), cols(x["L0_attn_bK"])], 1),
             np.stack([cols(qkvb[0:D]), cols(qkvb[D:2 * D])], 1)], 1)),
        "bv0": f(x["L0_attn_bV"]), "bv1": qkvb[2 * D:],
        "wo0": f(x["L0_attn_WO"]), "bo0": f(x["L0_attn_bO"]),
        "wo1": chunks(x["L1_attn_c_proj_w"]), "bo1": f(x["L1_attn_c_proj_b"]),
        "wr": chunks(x["L0_ffn_Wr"]), "br": f(x["L0_ffn_br"]),
        "w1": np.ascontiguousarray(f(x["L0_ffn_W1"]).reshape(E, KC, 128, HID).transpose(2, 0, 1, 3)),
        "w2": np.ascontiguousarray(f(x["L0_ffn_W2"]).reshape(E, HC, 128, D).transpose(2, 0, 1, 3)),
        "b1": f(x["L0_ffn_b1"]).reshape(-1), "b2": f(x["L0_ffn_b2"]).reshape(-1),
        "f1": chunks(f(x["L1_ffn_w1"]).T),
        "f2": chunks(f(x["L1_ffn_w2"]).T),
        "conv": np.ascontiguousarray(np.concatenate(
            [f(x["L1_ffn_conv_w"])[:, 0, :], f(x["L1_ffn_conv_b"])[:, None]], 1).reshape(HFC, 128, 4).transpose(1, 0, 2)),
    }


def kernel(**inputs):
    import concourse.bacc as bacc
    from concourse.bass_utils import run_bass_kernel_spmd

    nc = bacc.Bacc("TRN2", target_bir_lowering=False, num_devices=1)
    arrays = {f"in_{k}": np.ascontiguousarray(v) for k, v in laid_out(inputs).items()}
    aps = {k[3:]: nc.dram_tensor(k, v.shape, mybir.dt.from_np(v.dtype), kind="ExternalInput").ap()
           for k, v in arrays.items()}
    out = nc.dram_tensor("out", (B, T, D), F32, kind="ExternalOutput").ap()
    program(nc, aps, out)
    result = run_bass_kernel_spmd(nc, [arrays], core_ids=[0])
    return result.results[0]["out"]
```
